# Optimizing a Trainium2 kernel written in Bass

```python
import numpy as np
import jax
import jax.numpy as jnp

def _softmax(x, axis=-1):
    return jax.nn.softmax(x, axis=axis)

def _gelu(x):
    return jax.nn.gelu(x, approximate=True)

def _silu(x):
    return jax.nn.silu(x)

def _sigmoid(x):
    return jax.nn.sigmoid(x)

def _layernorm(x, axis=-1, eps=1e-05):
    m = jnp.mean(x, axis=axis, keepdims=True)
    v = jnp.var(x, axis=axis, keepdims=True)
    return (x - m) / jnp.sqrt(v + eps)

def _scatter_add(tgt, idx, src, axis=0):
    return tgt.at[idx].add(src)

def _segment_sum(src, seg, n):
    return jax.ops.segment_sum(src, seg, n)
kernel_name = 'mk_seq_postln_d1_jaxref_r8_36180f'

def setup_inputs(seed: int=0):
    np.random.seed(seed)
    _w = jnp.asarray

    def _L0_attn_setup():
        import jax, jax.numpy as jnp
        import numpy as np
        B, T, D = (2, 256, 128)
        HEAD_DIM, N_HEADS, N_HH, HEAD_V_DIM, CONV_SIZE = (128, 8, 3, 128, 4)

        def _short_conv(x, w):
            cs = w.shape[-1]
            t = x.shape[1]
            xp = jnp.pad(x, ((0, 0), (cs - 1, 0), (0, 0)))
            y = sum((xp[:, i:i + t, :] * w[:, i] for i in range(cs)))
            return jax.nn.silu(y)

        def _l2norm(x, eps=1e-06):
            return x * jax.lax.rsqrt(jnp.sum(x * x, -1, keepdims=True) + eps)

        def _forward(x, Wq, Wk, Wv, Wb, Wa, A_log, dt_bias, conv_q, conv_k, conv_v, Wg, rms_weight, Wo):
            b, t, _ = x.shape
            h, d, dv, nh = (N_HEADS, HEAD_DIM, HEAD_V_DIM, N_HH)
            q = _short_conv(x @ Wq, conv_q).reshape(b, t, h, d)
            k = _short_conv(x @ Wk, conv_k).reshape(b, t, nh, h, d).transpose(0, 1, 3, 2, 4)
            v = _short_conv(x @ Wv, conv_v).reshape(b, t, nh, h, dv).transpose(0, 1, 3, 2, 4)
            beta = 2.0 * jax.nn.sigmoid(x @ Wb).reshape(b, t, nh, h).transpose(0, 1, 3, 2)
            g = -jnp.exp(A_log) * jax.nn.softplus(x @ Wa + dt_bias)
            q = _l2norm(q) * d ** (-0.5)
            k = _l2norm(k)

            def step(S, inp):
                qt, kt, vt, bt, gt = inp
                S = S * jnp.exp(gt)[..., None, None]
                for i in range(nh):
                    ki, vi, bi = (kt[:, :, i], vt[:, :, i], bt[:, :, i])
                    kS = jnp.einsum('bhd,bhde->bhe', ki, S)
                    S = S + bi[..., None, None] * (ki[..., None] * (vi - kS)[:, :, None, :])
                o = jnp.einsum('bhd,bhde->bhe', qt, S)
                return (S, o)
            xs = tuple((jnp.moveaxis(a, 1, 0) for a in (q, k, v, beta, g)))
            S0 = jnp.zeros((b, h, d, dv), x.dtype)
            _, o = jax.lax.scan(step, S0, xs)
            o = jnp.moveaxis(o, 0, 1)
            gate = (x @ Wg).reshape(b, t, h, dv)
            o = o * jax.lax.rsqrt(jnp.mean(o * o, -1, keepdims=True) + 1e-05) * rms_weight
            o = o * jax.nn.silu(gate)
            return o.reshape(b, t, h * dv) @ Wo
        key = jax.random.key(seed)
        ks = jax.random.split(key, 16)
        h, d, dv, nh, cs = (N_HEADS, HEAD_DIM, HEAD_V_DIM, N_HH, CONV_SIZE)
        f = lambda k, shape, s=0.02: jax.random.normal(k, shape, jnp.float32) * s
        return {'x': f(ks[0], (B, T, D), 1.0), 'cos': f(ks[1], (T, d), 1.0), 'sin': f(ks[2], (T, d), 1.0), 'Wq': f(ks[3], (D, h * d)), 'Wk': f(ks[4], (D, h * d * nh)), 'Wv': f(ks[5], (D, h * dv * nh)), 'Wb': f(ks[6], (D, h * nh)), 'Wa': f(ks[7], (D, h)), 'A_log': jnp.log(jax.random.uniform(ks[8], (h,), jnp.float32, 0.5, 8.0)), 'dt_bias': f(ks[9], (h,), 0.1), 'conv_q': f(ks[10], (h * d, cs), 0.5), 'conv_k': f(ks[11], (h * d * nh, cs), 0.5), 'conv_v': f(ks[12], (h * dv * nh, cs), 0.5), 'Wg': f(ks[13], (D, h * dv)), 'rms_weight': jnp.ones((dv,), jnp.float32), 'Wo': f(ks[14], (h * dv, D))}
    _L0_attn_in = _L0_attn_setup()

    def _L0_ffn_setup():
        import jax, jax.numpy as jnp
        import numpy as np
        import math
        MAX_NORM = 0.95
        CURVATURE = 1.0
        TOP_K = 2
        EPS = 1e-07

        def _project_to_ball(x):
            norm = jnp.clip(jnp.linalg.norm(x, axis=-1, keepdims=True), EPS, None)
            scale = jnp.where(norm > MAX_NORM, MAX_NORM / norm, jnp.ones_like(norm))
            return x * scale
        key = jax.random.key(seed)
        ks = jax.random.split(key, 8)
        B, N, D, E, F = (2, 256, 128, 8, 512)
        x = jax.random.normal(ks[0], (B, N, D), dtype=jnp.float32)
        c = jax.random.normal(ks[1], (E, D), dtype=jnp.float32)
        centroids = c / jnp.linalg.norm(c, axis=-1, keepdims=True) * 0.5
        Wp = jax.random.normal(ks[2], (D, D), dtype=jnp.float32) * 0.02
        bp = jnp.zeros((D,), dtype=jnp.float32)
        W1 = jax.random.normal(ks[3], (E, D, F), dtype=jnp.float32) * 0.02
        b1 = jnp.zeros((E, F), dtype=jnp.float32)
        W2 = jax.random.normal(ks[4], (E, F, D), dtype=jnp.float32) * 0.02
        b2 = jnp.zeros((E, D), dtype=jnp.float32)
        return {'x': x, 'centroids': centroids, 'Wp': Wp, 'bp': bp, 'W1': W1, 'b1': b1, 'W2': W2, 'b2': b2}
    _L0_ffn_in = _L0_ffn_setup()
    _d = {'L0_attn_x': _L0_attn_in['x'], 'L0_attn_cos': _L0_attn_in['cos'], 'L0_attn_sin': _L0_attn_in['sin'], 'L0_attn_Wq': _L0_attn_in['Wq'], 'L0_attn_Wk': _L0_attn_in['Wk'], 'L0_attn_Wv': _L0_attn_in['Wv'], 'L0_attn_Wb': _L0_attn_in['Wb'], 'L0_attn_Wa': _L0_attn_in['Wa'], 'L0_attn_A_log': _L0_attn_in['A_log'], 'L0_attn_dt_bias': _L0_attn_in['dt_bias'], 'L0_attn_conv_q': _L0_attn_in['conv_q'], 'L0_attn_conv_k': _L0_attn_in['conv_k'], 'L0_attn_conv_v': _L0_attn_in['conv_v'], 'L0_attn_Wg': _L0_attn_in['Wg'], 'L0_attn_rms_weight': _L0_attn_in['rms_weight'], 'L0_attn_Wo': _L0_attn_in['Wo'], 'L0_ffn_centroids': _L0_ffn_in['centroids'], 'L0_ffn_Wp': _L0_ffn_in['Wp'], 'L0_ffn_bp': _L0_ffn_in['bp'], 'L0_ffn_W1': _L0_ffn_in['W1'], 'L0_ffn_b1': _L0_ffn_in['b1'], 'L0_ffn_W2': _L0_ffn_in['W2'], 'L0_ffn_b2': _L0_ffn_in['b2']}
    _x0 = _d['L0_attn_x']
    _d['L0_attn_x'] = jax.random.normal(jax.random.fold_in(jax.random.key(seed), 1), (8, 1024, 128), dtype=_x0.dtype)
    del _x0
    return _d

def reference(L0_attn_x, L0_attn_cos, L0_attn_sin, L0_attn_Wq, L0_attn_Wk, L0_attn_Wv, L0_attn_Wb, L0_attn_Wa, L0_attn_A_log, L0_attn_dt_bias, L0_attn_conv_q, L0_attn_conv_k, L0_attn_conv_v, L0_attn_Wg, L0_attn_rms_weight, L0_attn_Wo, L0_ffn_centroids, L0_ffn_Wp, L0_ffn_bp, L0_ffn_W1, L0_ffn_b1, L0_ffn_W2, L0_ffn_b2):

    def _L0_attn_ref(x, cos, sin, Wq, Wk, Wv, Wb, Wa, A_log, dt_bias, conv_q, conv_k, conv_v, Wg, rms_weight, Wo):
        import jax, jax.numpy as jnp
        import numpy as np
        B, T, D = (2, 256, 128)
        HEAD_DIM, N_HEADS, N_HH, HEAD_V_DIM, CONV_SIZE = (128, 8, 3, 128, 4)

        def _short_conv(x, w):
            cs = w.shape[-1]
            t = x.shape[1]
            xp = jnp.pad(x, ((0, 0), (cs - 1, 0), (0, 0)))
            y = sum((xp[:, i:i + t, :] * w[:, i] for i in range(cs)))
            return jax.nn.silu(y)

        def _l2norm(x, eps=1e-06):
            return x * jax.lax.rsqrt(jnp.sum(x * x, -1, keepdims=True) + eps)

        def _forward(x, Wq, Wk, Wv, Wb, Wa, A_log, dt_bias, conv_q, conv_k, conv_v, Wg, rms_weight, Wo):
            b, t, _ = x.shape
            h, d, dv, nh = (N_HEADS, HEAD_DIM, HEAD_V_DIM, N_HH)
            q = _short_conv(x @ Wq, conv_q).reshape(b, t, h, d)
            k = _short_conv(x @ Wk, conv_k).reshape(b, t, nh, h, d).transpose(0, 1, 3, 2, 4)
            v = _short_conv(x @ Wv, conv_v).reshape(b, t, nh, h, dv).transpose(0, 1, 3, 2, 4)
            beta = 2.0 * jax.nn.sigmoid(x @ Wb).reshape(b, t, nh, h).transpose(0, 1, 3, 2)
            g = -jnp.exp(A_log) * jax.nn.softplus(x @ Wa + dt_bias)
            q = _l2norm(q) * d ** (-0.5)
            k = _l2norm(k)

            def step(S, inp):
                qt, kt, vt, bt, gt = inp
                S = S * jnp.exp(gt)[..., None, None]
                for i in range(nh):
                    ki, vi, bi = (kt[:, :, i], vt[:, :, i], bt[:, :, i])
                    kS = jnp.einsum('bhd,bhde->bhe', ki, S)
                    S = S + bi[..., None, None] * (ki[..., None] * (vi - kS)[:, :, None, :])
                o = jnp.einsum('bhd,bhde->bhe', qt, S)
                return (S, o)
            xs = tuple((jnp.moveaxis(a, 1, 0) for a in (q, k, v, beta, g)))
            S0 = jnp.zeros((b, h, d, dv), x.dtype)
            _, o = jax.lax.scan(step, S0, xs)
            o = jnp.moveaxis(o, 0, 1)
            gate = (x @ Wg).reshape(b, t, h, dv)
            o = o * jax.lax.rsqrt(jnp.mean(o * o, -1, keepdims=True) + 1e-05) * rms_weight
            o = o * jax.nn.silu(gate)
            return o.reshape(b, t, h * dv) @ Wo
        return _forward(x, Wq, Wk, Wv, Wb, Wa, A_log, dt_bias, conv_q, conv_k, conv_v, Wg, rms_weight, Wo)

    def _L0_ffn_ref(x, centroids, Wp, bp, W1, b1, W2, b2):
        import jax, jax.numpy as jnp
        import numpy as np
        import math
        MAX_NORM = 0.95
        CURVATURE = 1.0
        TOP_K = 2
        EPS = 1e-07

        def _project_to_ball(x):
            norm = jnp.clip(jnp.linalg.norm(x, axis=-1, keepdims=True), EPS, None)
            scale = jnp.where(norm > MAX_NORM, MAX_NORM / norm, jnp.ones_like(norm))
            return x * scale
        B, N, D = x.shape
        E = centroids.shape[0]
        x_hyper = _project_to_ball(x @ Wp + bp)
        c_proj = _project_to_ball(centroids)
        x_norm_sq = jnp.sum(x_hyper * x_hyper, axis=-1)
        c_norm_sq = jnp.sum(c_proj * c_proj, axis=-1)
        x_norm_sq = jnp.clip(x_norm_sq, None, 0.99)
        c_norm_sq = jnp.clip(c_norm_sq, None, 0.99)
        dot = jnp.einsum('bnd,ed->bne', x_hyper, c_proj)
        diff_sq = jnp.maximum(x_norm_sq[..., None] + c_norm_sq - 2.0 * dot, 0.0)
        denom = (1.0 - x_norm_sq)[..., None] * (1.0 - c_norm_sq) + EPS
        arg = jnp.clip(1.0 + 2.0 * diff_sq / denom, 1.0 + EPS, None)
        dist = jnp.arccosh(arg)
        routing_logits = -dist / math.sqrt(CURVATURE)
        top_v, top_i = jax.lax.top_k(routing_logits, TOP_K)
        top_w = jax.nn.softmax(top_v, axis=-1)
        comb = jnp.sum(jax.nn.one_hot(top_i, E, dtype=x.dtype) * top_w[..., None], axis=2)
        h = jax.nn.gelu(jnp.einsum('bnd,edf->bnef', x, W1) + b1, approximate=False)
        y = jnp.einsum('bnef,efd->bned', h, W2) + b2
        out = jnp.einsum('bne,bned->bnd', comb, y)
        return out
    x = L0_attn_x
    x = _layernorm(x + _L0_attn_ref(x, L0_attn_cos, L0_attn_sin, L0_attn_Wq, L0_attn_Wk, L0_attn_Wv, L0_attn_Wb, L0_attn_Wa, L0_attn_A_log, L0_attn_dt_bias, L0_attn_conv_q, L0_attn_conv_k, L0_attn_conv_v, L0_attn_Wg, L0_attn_rms_weight, L0_attn_Wo), axis=-1)
    x = _layernorm(x + _L0_ffn_ref(x, L0_ffn_centroids, L0_ffn_Wp, L0_ffn_bp, L0_ffn_W1, L0_ffn_b1, L0_ffn_W2, L0_ffn_b2), axis=-1)
    return x

_drawn_inputs = setup_inputs


def setup_inputs(seed=0):
    import zlib

    import numpy as np

    out = dict(_drawn_inputs(seed))
    spreads = {'L0_attn_rms_weight': (1.0, 0.6),
     'L0_ffn_bp': (0.0, 0.1),
     'L0_ffn_b1': (0.0, 0.45),
     'L0_ffn_b2': (0.0, 0.1)}
    factors = {'L0_attn_Wb': 8.0, 'L0_attn_Wa': 43.089, 'L0_attn_A_log': 4.306, 'L0_attn_dt_bias': 141.49}
    for name, (base, spread) in spreads.items():
        noise = np.random.default_rng([zlib.crc32(name.encode()), seed]).standard_normal(out[name].shape)
        drawn = base * np.exp(spread * noise) if base else spread * noise
        out[name] = jnp.asarray(drawn.astype(out[name].dtype))
    for name, factor in factors.items():
        out[name] = (out[name] * factor).astype(out[name].dtype)
    return out
```

```python
from contextlib import ExitStack

import concourse.bass as bass
from concourse import mybir

ALU = mybir.AluOpType
ACT = mybir.ActivationFunctionType
AX = mybir.AxisListType
F32 = mybir.dt.float32

P = 128
NB, NT = 8, 1024
NHEAD = 8
NHH = 3
TAPS = 4
HALO = TAPS - 1
CT = 32
R = CT * NHH
LH = 4
NL = NHEAD // LH
NSC = NB * NT // P
CPS = P // CT
NCH = NSC * CPS
TILES = NHEAD * (1 + 2 * NHH)
SLOTS = 14
assert SLOTS * CPS == TILES

STAGES = ["X", "W0", "H", "H2", "X", "W1", "H", "H1", "H2", "X", "W2", "H", "H1", "H2"]
assert len(STAGES) == SLOTS

EPS_L2 = 1e-6
EPS_RMS = 1e-5
EPS_LN = 1e-5
NE, FF = 8, 512
FC = NE * FF // P
FT = 512
FQ = FT // P
MAX_NORM = 0.95


def need(eng, sem, value):
    if isinstance(value, int) and value <= 0:
        return
    eng.wait_ge(sem, value)


def known(value, low, high):
    return not isinstance(value, int) or low <= value < high


def over(ap, shape, axis):
    return ap.unsqueeze(axis).broadcast_to(shape)


def tile_of(m):
    nv = NHH * NHEAD
    if m < nv:
        return "v", m % NHH, m // NHH
    m -= nv
    if m < nv:
        return "k", m % NHH, m // NHH
    return "q", 0, m - nv


def attn_consts():
    import numpy as np
    row = np.arange(P)
    tok, step = row % CT, row // CT
    k = np.arange(CT)
    after = (k[:, None] > tok[None, :]).astype(np.float32)
    upto = (k[:, None] <= tok[None, :]).astype(np.float32)
    when = NHH * tok + step
    j, i = when[:R, None], when[None, :R]
    earlier = np.zeros((R, P), np.float32)
    earlier[:, :R] = j < i
    earlier[:, R:] = tok[:R, None] <= tok[None, R:]
    first = -((j // 2 == i // 2) & (j < i)).astype(np.float32)
    merge = [((j // b != i // b) & (j // (b * r) == i // (b * r)) & (i < j)).astype(np.float32)
             for b, r in ((2, 3), (6, 4), (24, 4))]
    padr = lambda a: np.concatenate([a, np.zeros((P - a.shape[0], a.shape[1]), np.float32)], 0)
    padl = lambda a: np.concatenate([np.zeros((R, P), np.float32), a], 0)
    ident = np.eye(P, dtype=np.float32)
    sign = np.where(row < R, -1.0, 1.0).astype(np.float32)[:, None]
    keep = np.ones((P, NSC), np.float32)
    keep[:, ::NT // P] = 0.0
    e = np.arange(NE)
    lower = (e[None, :] < e[:, None]).astype(np.float32).reshape(1, NE * NE).repeat(P, 0)
    return np.concatenate([ident, padl(after), padl(upto), padr(earlier), padr(first)]
                          + [padr(m) for m in merge] + [sign, keep, lower], 1)


C_ID, C_AFTER, C_UPTO, C_EARLY, C_FIRST = 0, P, 2 * P, 3 * P, 4 * P
C_MERGE = C_FIRST + R
C_SIGN = C_MERGE + 3 * R
C_KEEP = C_SIGN + 1
C_LOWER = C_KEEP + NSC
C_ALL = C_LOWER + NE * NE


def attention_part(nc, x, Wq, Wk, Wv, Wb, Wa, A_log, dt_bias, conv_q, conv_k, conv_v, Wg, rms_weight, Wo,
                   consts, x1):
    ctx = ExitStack()
    with ctx:
        def sb(name, shape):
            return ctx.enter_context(nc.sbuf_tensor(name, shape, F32))

        def pb(name, shape):
            return ctx.enter_context(nc.psum_tensor(name, shape, F32))

        def sem(name):
            return ctx.enter_context(nc.semaphore(name))

        def sems(name, n=NL):
            return [sem(f"{name}{k}") for k in range(n)]

        xf = x.rearrange("b t d -> (b t) d")

        C = sb("C", [P, C_ALL])
        ident = C[:, C_ID:C_ID + P]
        after = C[R:P, C_AFTER:C_AFTER + R]
        upto = C[R:P, C_UPTO:C_UPTO + P]
        earlier = C[0:R, C_EARLY:C_EARLY + P]
        first = C[0:R, C_FIRST:C_FIRST + R]
        merge = [C[0:R, C_MERGE + R * m:C_MERGE + R * m + R] for m in range(3)]
        sign = C[:, C_SIGN:C_SIGN + 1]
        WQ = sb("WQ", [P, NHEAD, P])
        WK = sb("WK", [P, NHH * NHEAD, P])
        WV = sb("WV", [P, NHH * NHEAD, P])
        WG = sb("WG", [P, NHEAD * P])
        WO = sb("WO", [P, NHEAD, P])
        CWQ = sb("CWQ", [P, NHEAD, TAPS])
        CWK = sb("CWK", [P, NHH * NHEAD, TAPS])
        CWV = sb("CWV", [P, NHH * NHEAD, TAPS])
        rms = sb("rms", [P, 1])
        half4 = sb("half4", [P, NHEAD])
        mhalf = sb("mhalf", [P, NHEAD])
        ones = sb("ones", [P, P])

        BETA = sb("BETA", [P, NCH, NHEAD])
        TAIL = sb("TAIL", [P, NCH, NHEAD])
        HEADD = sb("HEADD", [P, NCH, NHEAD])
        WHOLE = sb("WHOLE", [P, NCH, NHEAD])
        G = TAIL

        pctx = ExitStack()
        with pctx:
            def psb(name, shape):
                return pctx.enter_context(nc.sbuf_tensor(name, shape, F32))
            XL = psb("XL", [P, 2, 4, P])
            XLT = psb("XLT", [P, 2, 4 * P])
            RAW = psb("RAW", [P, 2, 16, CT])
            WALL = psb("WALL", [P, 4, CT])
            AEXP = psb("AEXP", [P, NHEAD])
            DTB = psb("DTB", [P, NHEAD])
            Y = psb("Y", [P, NCH, NHEAD])
            U_ = psb("U_", [P, NCH, NHEAD])
            Z = psb("Z", [P, NCH, NHEAD])
            Z2 = psb("Z2", [P, NCH, NHEAD])
            PXT = pctx.enter_context(nc.psum_tensor("PXT", [P, 2, 512], F32))
            PRW = pctx.enter_context(nc.psum_tensor("PRW", [P, 2, 512], F32))
            PTB = pctx.enter_context(nc.psum_tensor("PTB", [P, 2, 512], F32))
            w_in, wz, prep = sem("w_in"), sem("wz"), sem("prep")
            xl_in = sems("xl_in", 2)
            xlt_ps, xlt_sb, raw_ps, raw_sb, aw_sb, bt_sb = (sem(n) for n in (
                "xlt_ps", "xlt_sb", "raw_ps", "raw_sb", "aw_sb", "bt_sb"))
            tv, ta, tab_ps, tab_sb = sem("tv"), sem("ta"), sem("tab_ps"), sem("tab_sb")
            NLOAD = NB * NT // 512
            flat = lambda t: t[:, :, :].rearrange("p a b -> p (a b)")
            NW = 19
            with nc.Block() as block:
                @block.sync
                def _(sp):
                    sp.dma_start(C[:, :], consts).then_inc(w_in, 16)
                    sp.wait_ge(wz, 1)
                    for g in range(4):
                        if g < NHH:
                            sp.dma_start(WALL[:, g, 0:NHEAD], Wb[:, g * NHEAD:(g + 1) * NHEAD]).then_inc(w_in, 16)
                        sp.dma_start(WALL[:, g, NHEAD:2 * NHEAD], Wa).then_inc(w_in, 16)
                    sp.dma_start(AEXP[:, :], A_log.partition_broadcast(P)).then_inc(w_in, 16)
                    sp.dma_start(DTB[:, :], dt_bias.partition_broadcast(P)).then_inc(w_in, 16)
                    for u in range(2):
                        sp.dma_start(XL[:, u], xf[512 * u:512 * (u + 1)].rearrange("(q p) d -> p q d", p=P)).then_inc(xl_in[u], 16)
                    sp.dma_start(WQ[:, :, :], Wq.rearrange("d (h c) -> d h c", c=P)).then_inc(w_in, 16)
                    sp.dma_start(WK[:, :, :], Wk.rearrange("d (h c) -> d h c", c=P)).then_inc(w_in, 16)
                    sp.dma_start(WV[:, :, :], Wv.rearrange("d (h c) -> d h c", c=P)).then_inc(w_in, 16)
                    sp.dma_start(WG[:, :], Wg).then_inc(w_in, 16)
                    sp.dma_start(WO[:, :, :], Wo.rearrange("(h e) d -> e h d", e=P)).then_inc(w_in, 16)
                    sp.dma_start(CWQ[:, :, :], conv_q.rearrange("(h c) t -> c h t", c=P)).then_inc(w_in, 16)
                    sp.dma_start(CWK[:, :, :], conv_k.rearrange("(h c) t -> c h t", c=P)).then_inc(w_in, 16)
                    sp.dma_start(CWV[:, :, :], conv_v.rearrange("(h c) t -> c h t", c=P)).then_inc(w_in, 16)
                    sp.dma_start(rms[:, :], rms_weight.unsqueeze(1)).then_inc(w_in, 16)
                    with sp.Fori(1, NLOAD // 2) as t:
                        for b in range(2):
                            sp.wait_ge(xlt_ps, 2 * t + b - 1)
                            sp.dma_start(XL[:, b], xf[bass.ds((2 * t + b) * 512, 512)].rearrange("(q p) d -> p q d", p=P)).then_inc(xl_in[b], 16)

                @block.gpsimd
                def _(pool):
                    pool.memset(WALL[:, :, :], 0.0).then_inc(wz, 1)
                    pool.memset(ones[:, :], 1.0).then_inc(wz, 1)
                    pool.memset(half4[:, :], 0.5).then_inc(wz, 1)
                    pool.memset(mhalf[:, :], -0.5).then_inc(wz, 1)

                @block.tensor
                def _(pe):
                    pe.wait_ge(w_in, 16 * NW)
                    with pe.Fori(0, NLOAD // 2) as t:
                        for b in range(2):
                            n = 2 * t + b
                            pe.wait_ge(xl_in[b], 16 * (t + 1))
                            for q in range(4):
                                mm = pe.transpose(PXT[:, b, q * P:(q + 1) * P], XL[:, b, q], ident)
                            mm.then_inc(xlt_ps, 1)
                            pe.wait_ge(xlt_sb, n + 1)
                            pe.wait_ge(raw_sb, n)
                            pe.matmul(PRW[:, b], WALL[:, :, :], XLT[:, b], start=True, stop=True).then_inc(raw_ps, 1)
                    pe.wait_ge(wz, 4)
                    pe.wait_ge(tv, 15)
                    for k in range(12):
                        lhs = (upto, after, ones[R:P, :])[k % 3]
                        m = R if k % 3 == 1 else P
                        piece = flat(G)[R:P, 512 * (k // 3):512 * (k // 3) + 512]
                        if k >= 2:
                            pe.wait_ge(tab_sb, k - 1)
                        pe.matmul(PTB[0:m, k % 2], lhs, piece, start=True, stop=True).then_inc(tab_ps, 1)

                @block.scalar
                def _(act):
                    act.wait_ge(w_in, 16 * NW)
                    act.activation(AEXP[:, :], AEXP[:, :], ACT.Exp).then_inc(ta, 1)
                    with act.Fori(0, NLOAD // 2) as t:
                        for b in range(2):
                            n = 2 * t + b
                            act.wait_ge(xlt_ps, n + 1)
                            act.activation(XLT[:, b], PXT[:, b], ACT.Copy).then_inc(xlt_sb, 1)
                            act.wait_ge(raw_sb, n + 1)
                            act.activation(BETA[:, bass.ds(n * 16, 16), :], RAW[:, b, :, 0:NHEAD], ACT.Tanh, scale=0.5).then_inc(bt_sb, 1)
                    act.wait_ge(tv, 1)
                    act.activation(flat(U_), flat(U_), ACT.Exp, scale=-1.0).then_inc(ta, 1)
                    for k in range(12):
                        to = (HEADD, TAIL, WHOLE)[k % 3]
                        m = R if k % 3 == 1 else P
                        act.wait_ge(tab_ps, k + 1)
                        act.activation(flat(to)[0:m, 512 * (k // 3):512 * (k // 3) + 512], PTB[0:m, k % 2], ACT.Exp).then_inc(tab_sb, 1)

                @block.vector
                def _(dve):
                    dve.wait_ge(w_in, 16 * NW)
                    with dve.Fori(0, NLOAD // 2) as t:
                        for b in range(2):
                            n = 2 * t + b
                            dve.wait_ge(raw_ps, n + 1)
                            dve.wait_ge(bt_sb, n)
                            dve.transpose(RAW[:, b].rearrange("p a b -> p (a b)"), PRW[:, b]).then_inc(raw_sb, 1)
                            dve.wait_ge(raw_sb, n + 1)
                            dve.tensor_tensor(Y[:, bass.ds(n * 16, 16), :], RAW[:, b, :, NHEAD:2 * NHEAD],
                                              over(DTB[:, :], [P, 16, NHEAD], 1), ALU.add).then_inc(aw_sb, 1)
                    y, u, z, z2, g = flat(Y), flat(U_), flat(Z), flat(Z2), flat(G)
                    dve.wait_ge(aw_sb, NLOAD)
                    dve.scalar_tensor_tensor(u, y, -1.0, y, ALU.mult, ALU.max).then_inc(tv, 1)
                    dve.wait_ge(ta, 2)
                    dve.tensor_scalar(z2, u, 2.0, None, ALU.add).then_inc(tv, 1)
                    dve.wait_ge(tv, 2)
                    dve.reciprocal(z, z2).then_inc(tv, 1)
                    dve.wait_ge(tv, 3)
                    dve.tensor_tensor(z, z, u, ALU.mult).then_inc(tv, 1)
                    dve.wait_ge(tv, 4)
                    dve.tensor_tensor(z2, z, z, ALU.mult).then_inc(tv, 1)
                    dve.wait_ge(tv, 5)
                    dve.tensor_scalar(g, z2, 1.0 / 15, None, ALU.mult).then_inc(tv, 1)
                    for s, c in enumerate((13, 11, 9, 7, 5, 3)):
                        dve.wait_ge(tv, 6 + s)
                        dve.scalar_tensor_tensor(g, g, 1.0 / c, z2, ALU.add, ALU.mult).then_inc(tv, 1)
                    dve.wait_ge(tv, 12)
                    dve.scalar_tensor_tensor(g, g, 1.0, z, ALU.add, ALU.mult).then_inc(prep, 1)
                    dve.tensor_scalar(y, y, 0.0, None, ALU.max).then_inc(prep, 1)
                    dve.wait_ge(prep, 2)
                    dve.scalar_tensor_tensor(g, g, 2.0, y, ALU.mult, ALU.add).then_inc(prep, 1)
                    dve.tensor_scalar(AEXP[:, :], AEXP[:, :], -1.0, None, ALU.mult).then_inc(prep, 1)
                    dve.wait_ge(prep, 4)
                    dve.tensor_tensor(G[:, :, :], G[:, :, :], over(AEXP[:, :], [P, NCH, NHEAD], 1), ALU.mult).then_inc(tv, 1)
                    dve.wait_ge(tv, 13)
                    firsts = G[R:R + 1, 0:NCH:NT // CT, :]
                    dve.tensor_scalar(firsts, firsts, -30000.0, None, ALU.add).then_inc(tv, 2)
                    dve.wait_ge(bt_sb, NLOAD)
                    dve.tensor_scalar(flat(BETA), flat(BETA), 1.0, None, ALU.add).then_inc(prep, 1)
                    dve.tensor_scalar(CWQ[:, :, :], CWQ[:, :, :], 0.5, None, ALU.mult)
                    dve.tensor_scalar(CWK[:, :, :], CWK[:, :, :], 0.5, None, ALU.mult)
                    dve.tensor_scalar(CWV[:, :, :], CWV[:, :, :], 0.5, None, ALU.mult)
                    dve.tensor_scalar(WO[:, :, :], WO[:, :, :], rms[:, 0:1], 0.5, ALU.mult, ALU.mult)
                    dve.wait_ge(prep, 5)
                    dve.wait_ge(tab_sb, 12)
                    dve.tensor_scalar(flat(HEADD), flat(HEADD), sign, None, ALU.mult)
                    dve.tensor_tensor(flat(TAIL)[0:R], flat(TAIL)[0:R], flat(BETA)[0:R], ALU.mult).then_inc(prep, 1)
                    dve.wait_ge(prep, 6)

        XR = sb("XR", [P, 2, P])
        XRES = sb("XRES", [P, 2, P])
        XT = sb("XT", [P, 2, HALO + P])
        KQ = sb("KQ", [P, 2, NHEAD, CPS, P])
        VT = sb("VT", [P, 2, NHEAD, CPS, R])
        CY = sb("CY", [P, 4, P])
        CTH = sb("CTH", [P, 4, P])
        SQ = sb("SQ", [P, NL, LH, P])
        SSE = sb("SSE", [P, NL, LH])
        QSE = sb("QSE", [P, 2, NHEAD])
        RT = sb("RT", [P, NL, LH])
        R2 = sb("R2", [P, NL, LH])
        S1 = sb("S1", [P, NL, LH])
        KDS = sb("KDS", [P, NL, LH])
        GM = sb("GM", [P, NL, LH, CT])
        EX = sb("EX", [R, NL, LH, CT])
        E2 = sb("E2", [R, NL, LH, CT])
        EM = SQ
        U = sb("U", [P, NL, 2, LH, P])
        KD = sb("KD", [R, NL, 2, LH, P])
        VP = sb("VP", [P, NL, 2, LH, P])
        Y1 = sb("Y1", [R, NL, LH, R])
        XB = sb("XB", [R, NL, LH, R])
        WB = sb("WB", [R, NL, LH, R])
        T0 = sb("T0", [R, NL, LH, R])
        T1 = sb("T1", [R, NL, LH, R])
        Y2 = sb("Y2", [R, NL, LH, R])
        Y3 = sb("Y3", [R, NL, LH, R])
        YF = sb("YF", [R, NL, LH, R])
        BZ = sb("BZ", [P, NL, LH, P])
        S = sb("S", [P, NHEAD, P])
        GSIL = sb("GSIL", [P, 2, NHEAD, P])
        SSO = sb("SSO", [P, NHEAD])
        FA = sb("FA", [P, NHEAD])
        FB = sb("FB", [P, NHEAD])
        OG = sb("OG", [P, NHEAD, P])
        GT = OG
        OGT = sb("OGT", [P, NHEAD, P])
        YL = sb("YL", [P, P])
        ST = sb("ST", [P, 6])
        MV = sb("MV", [P, 2])
        RS = sb("RS", [P, 1])
        X1 = sb("X1", [P, 2, P])
        spare = sb("spare", [P, 1])

        PO = pb("PO", [P, NHEAD, P])
        PP = pb("PP", [P, 2, 512])
        PI = pb("PI", [P, NL, 512])
        PG = pb("PG", [P, NL, 512])
        pgh = lambda l, m=P: PG[0:m, l].rearrange("p (h c) -> p h c", h=LH)
        inv = lambda l: PI[0:R, l, 0:LH * R].rearrange("p (h c) -> p h c", h=LH)
        PSS = [PG[:, l, LH * CT:LH * CT + LH] for l in range(NL)]
        PSQ = [PG[:, l, LH * CT + LH:LH * CT + 2 * LH] for l in range(NL)]
        PD = [PG[0:R, l, 0:LH * CT] for l in range(NL)]
        ptile = lambda m: PP[:, m % 2, 0:HALO + P]

        ready = sem("ready")
        READY = 2 + NL * 2 * (1 + LH)
        xr_in, xres_in, x1_out = sems("xr_in", 2), sems("xres_in", 2), sems("x1_out", 2)
        xt_ps, xt_sb, proj_ps, tap0_sb, taps_sb, tanh_sb, kqv_sb = (sem(n) for n in (
            "xt_ps", "xt_sb", "proj_ps", "tap0_sb", "taps_sb", "tanh_sb", "kqv_sb"))
        (sq_sb, ss_ps, gm_sb, e_sb, sse_sb, r2_sb, rt_sb, s1_sb, kds_sb, e2_sb, em_sb, seed_sb, y1_sb,
         kk_ps, u_sb, kr_ps, kd_sb, vr_ps, vp_sb, ks_ps, b_sb, z_ps, z_sb, o_ps, s_ps, s_sb, inv_ps, inv_sb,
         gate_ps, gt_sb, gsil_sb, ogt_ps, ogt_sb) = (sems(n) for n in (
             "sq_sb", "ss_ps", "gm_sb", "e_sb", "sse_sb", "r2_sb", "rt_sb", "s1_sb", "kds_sb", "e2_sb",
             "em_sb", "seed_sb", "y1_sb", "kk_ps", "u_sb", "kr_ps", "kd_sb", "vr_ps", "vp_sb", "ks_ps", "b_sb",
             "z_ps", "z_sb", "o_ps", "s_ps", "s_sb", "inv_ps", "inv_sb", "gate_ps", "gt_sb", "gsil_sb",
             "ogt_ps", "ogt_sb"))
        sso_sb, fa_sb, fb_sb, og_sb, wo_ps, y_sb, st_sb, mv_sb, rs_sb, x1_sb = (sem(n) for n in (
            "sso_sb", "fa_sb", "fb_sb", "og_sb", "wo_ps", "y_sb", "st_sb", "mv_sb", "rs_sb", "x1_sb"))

        def all_steps(eng, program):
            for i in range(2):
                for c in range(CPS):
                    program(i, i, c)
            with eng.Fori(1, NSC // 2) as t:
                for half in range(2):
                    for c in range(CPS):
                        program(2 * t + half, half, c)
            for i in range(NSC, NSC + 2):
                for c in range(CPS):
                    program(i, i % 2, c)

        def stage_bufs(k, l):
            base = (Y1, Y1, Y1, Y1, Y2, Y2, Y2, Y2, Y2, Y3, Y3, Y3, Y3, Y3)[k]
            kind = STAGES[k]
            if kind == "H":
                return base, base, T0
            if kind == "H1":
                return base, T0, T1
            if kind == "H2":
                return base, (T0 if k == 3 else T1), {3: Y2, 8: Y3, 13: YF}[k]
            return base, None, None

        def lagged(i, half, m):
            return (i - 1, 1 - half, m + TILES) if m < 0 else (i, half, m)

        def tile_known(i):
            return known(i, 0, NSC)

        with nc.Block() as block:
            @block.sync
            def _(sp):
                def rows(i):
                    return xf[bass.ds(i * P, P)] if not isinstance(i, int) else xf[i * P:(i + 1) * P]

                def out_rows(i):
                    return x1[bass.ds(i * P, P)] if not isinstance(i, int) else x1[i * P:(i + 1) * P]

                def program(i, half, c):
                    if c == 0 and known(i + 1, 1, NSC):
                        need(sp, xt_ps, i)
                        sp.dma_start(XR[:, 1 - half], rows((i + 1) % NSC)).then_inc(xr_in[1 - half], 16)
                    if c == 1 and known(i - 2, 0, NSC):
                        need(sp, y_sb, i - 2)
                        sp.dma_start(XRES[:, half], rows(i - 2)).then_inc(xres_in[half], 16)
                    if c == 3 and known(i - 2, 0, NSC):
                        sp.wait_ge(x1_sb, i - 1)
                        sp.dma_start(out_rows(i - 2), X1[:, half]).then_inc(x1_out[half], 16)

                sp.dma_start(XR[:, 0], rows(0)).then_inc(xr_in[0], 16)
                all_steps(sp, program)
                for b in range(2):
                    sp.wait_ge(x1_out[b], 16 * (NSC // 2))

            @block.tensor
            def _(pe):
                def transpose_x(i, half):
                    pe.wait_ge(xr_in[half], 16 * ((i + 2 - half) // 2) if isinstance(i, int) else 8 * (i + 2 - half))
                    pe.transpose(PG[:, 0, 0:P], XR[:, half], ident).then_inc(xt_ps, 1)

                def project(i, half, m):
                    kind, hh, h = tile_of(m)
                    T = TILES * i + m
                    if m == 0:
                        pe.wait_ge(xt_sb, 2 * i + 2)
                    need(pe, taps_sb, 3 * (T - 1))
                    w = {"q": WQ[:, h], "k": WK[:, hh * NHEAD + h], "v": WV[:, hh * NHEAD + h]}[kind]
                    pe.matmul(ptile(m), w, XT[:, half], start=True, stop=True).then_inc(proj_ps, 1)

                def invert(w, par, k, l):
                    kind = STAGES[k]
                    need(pe, inv_sb[l], SLOTS * w + k)
                    if k == 0:
                        pe.wait_ge(y1_sb[l], w + 1)
                    base, term, _ = stage_bufs(k, l)
                    for h in range(LH):
                        if kind == "X":
                            mm = pe.transpose(inv(l)[:, h], base[:, l, h], ident[0:R, 0:R])
                        elif kind[0] == "W":
                            mm = pe.matmul(inv(l)[:, h], U[0:R, l, par, h, 0:R], XB[:, l, h], start=True, stop=True)
                        else:
                            mm = pe.matmul(inv(l)[:, h], WB[:, l, h], term[:, l, h], start=True, stop=True)
                    mm.then_inc(inv_ps[l], 1)

                def program(i, half, c):
                    n = 4 * i + c
                    prep, invn, run = n - 4, n - 5, n - 6
                    sc = (1 - half)
                    rc, rs = (c - 2) % 4, (half if c < 2 else 1 - half)
                    do_prep, do_inv, do_run = (known(w, 0, NCH) for w in (prep, invn, run))
                    for k in range(SLOTS):
                        if do_inv:
                            for l in range(NL):
                                invert(invn, (c + 1) % 2, k, l)
                        if tile_known(i):
                            project(i, half, SLOTS * c + k)
                        if do_run and k == 0:
                            for l in range(NL):
                                need(pe, vp_sb[l], run + 2 if not isinstance(run, int) else min(run + 2, NCH))
                                need(pe, s_sb[l], run)
                                for h in range(LH):
                                    mm = pe.matmul(pgh(l)[:, h], KQ[:, rs, l * LH + h, rc], S[:, l * LH + h], start=True, stop=True)
                                mm.then_inc(ks_ps[l], 1)
                        if do_run and k == 2:
                            for l in range(NL):
                                pe.wait_ge(inv_sb[l], SLOTS * (run + 1))
                                pe.wait_ge(b_sb[l], run + 1)
                                for h in range(LH):
                                    mm = pe.matmul(pgh(l, R)[:, h], YF[:, l, h], BZ[0:R, l, h], start=True, stop=True)
                                mm.then_inc(z_ps[l], 1)
                        if do_run and k == 4:
                            for l in range(NL):
                                pe.wait_ge(z_sb[l], run + 1)
                                if rc == 0:
                                    need(pe, og_sb, i - 1)
                                for h in range(LH):
                                    mm = pe.matmul(PO[CT * rc:CT * rc + CT, l * LH + h], U[:, l, c % 2, h, R:P], BZ[:, l, h],
                                                   start=True, stop=True)
                                mm.then_inc(o_ps[l], 1)
                        if c == 2 and known(i - 2, 0, NSC):
                            if k == 3:
                                pe.wait_ge(og_sb, i - 1)
                                for l in range(NL):
                                    need(pe, z_sb[l], run + 1 if not isinstance(run, int) else min(run + 1, NCH))
                                    for h in range(LH):
                                        mm = pe.transpose(pgh(l)[:, h], OG[:, l * LH + h], ident)
                                    mm.then_inc(ogt_ps[l], 1)
                            if k == 5:
                                for l in range(NL):
                                    pe.wait_ge(ogt_sb[l], i - 1)
                                for h in range(NHEAD):
                                    mm = pe.matmul(PG[:, 0, 0:P], OGT[:, h], WO[:, h], start=(h == 0), stop=(h == NHEAD - 1))
                                mm.then_inc(wo_ps, 1)
                        if do_run and k == (6 if c == 2 else 5):
                            for l in range(NL):
                                if c == 2 and l == 0 and known(i - 2, 0, NSC):
                                    pe.wait_ge(y_sb, i - 1)
                                for h in range(LH):
                                    mm = pe.matmul(pgh(l)[:, h], KD[:, l, c % 2, h], BZ[0:R, l, h], start=True, stop=True)
                                mm.then_inc(s_ps[l], 1)
                        if c == 3 and k == 6 and known(i, 0, NSC):
                            for l in range(NL):
                                if do_run:
                                    pe.wait_ge(s_sb[l], run + 1)
                                elif do_prep:
                                    need(pe, vp_sb[l], prep)
                                pe.matmul(PG[:, l], XT[:, half, HALO:], WG[:, l * 512:(l + 1) * 512], start=True, stop=True).then_inc(gate_ps[l], 1)
                        if do_prep and k == 7:
                            for l in range(NL):
                                need(pe, vp_sb[l], prep)
                                if do_run:
                                    pe.wait_ge(s_sb[l], run + 1)
                                if c == 3 and known(i, 0, NSC):
                                    pe.wait_ge(gsil_sb[l], i + 1)
                                if c == 2 and l == 0 and known(i - 2, 0, NSC):
                                    pe.wait_ge(y_sb, i - 1)
                                pe.wait_ge(sq_sb[l], prep + 1)
                                pe.wait_ge(gm_sb[l], prep + 1)
                                pe.matmul(PD[l], after, GM[R:P, l], start=True, stop=True)
                                for h in range(LH):
                                    pe.matmul(PSS[l][:, h:h + 1], SQ[:, l, h], ones[:, 0:1], start=True, stop=True)
                                    mm = pe.matmul(PSQ[l][CT * c:CT * c + CT, h:h + 1], SQ[:, l, h, R:P], ones[:, 0:1], start=True, stop=True)
                                mm.then_inc(ss_ps[l], 1)
                        if c == 3 and k == 8 and known(i + 1, 1, NSC):
                            if do_prep:
                                pe.wait_ge(sse_sb[0], 2 * prep + 2)
                            else:
                                pe.wait_ge(gsil_sb[0], i + 1)
                            transpose_x(i + 1, 1 - half)
                        if do_prep and k == 9:
                            for l in range(NL):
                                pe.wait_ge(sse_sb[l], 2 * prep + 2)
                                if c == 3 and l == 0 and known(i + 1, 1, NSC):
                                    pe.wait_ge(xt_sb, 2 * i + 3)
                                for h in range(LH):
                                    kq = KQ[:, sc, l * LH + h, c]
                                    mm = pe.matmul(pgh(l, R)[:, h], kq[:, 0:R], kq, start=True, stop=True)
                                mm.then_inc(kk_ps[l], 1)
                        if do_prep and k == 11:
                            for l in range(NL):
                                pe.wait_ge(u_sb[l], prep + 1)
                                for h in range(LH):
                                    mm = pe.transpose(pgh(l, R)[:, h], KQ[:, sc, l * LH + h, c, 0:R], ident)
                                mm.then_inc(kr_ps[l], 1)
                        if do_prep and k == 12:
                            for l in range(NL):
                                pe.wait_ge(kd_sb[l], prep + 1)
                                for h in range(LH):
                                    mm = pe.transpose(pgh(l, R)[:, h], VT[:, sc, l * LH + h, c], ident)
                                mm.then_inc(vr_ps[l], 1)

                pe.wait_ge(ready, READY)
                transpose_x(0, 0)
                all_steps(pe, program)

            @block.scalar
            def _(act):
                def program(i, half, c):
                    n = 4 * i + c
                    prep, invn, run = n - 4, n - 5, n - 6
                    do_prep, do_inv, do_run = (known(w, 0, NCH) for w in (prep, invn, run))
                    for k in range(SLOTS):
                        if c == 2 and k == 0 and known(i - 2, 0, NSC):
                            for l in range(NL):
                                need(act, o_ps[l], run)
                            need(act, fa_sb, 2 * (i - 2))
                            need(act, wo_ps, i - 2)
                            for h in range(NHEAD):
                                op = act.activation(OGT[:, h], PO[:, h], ACT.Square, accum_out=SSO[:, h:h + 1])
                            op.then_inc(sso_sb, 1)
                        j, jh, m = lagged(i, half, SLOTS * c + k - 2)
                        if tile_known(j):
                            T = TILES * j + m
                            act.wait_ge(taps_sb, 3 * (T + 1))
                            act.activation(CTH[:, m % 4], CY[:, m % 4], ACT.Tanh).then_inc(tanh_sb, 1)
                        if do_inv and STAGES[k] == "X":
                            for l in range(NL):
                                act.wait_ge(inv_ps[l], SLOTS * invn + k + 1)
                                act.activation(XB[:, l], inv(l), ACT.Copy).then_inc(inv_sb[l], 1)
                        if do_run and k == 2:
                            for l in range(NL):
                                act.wait_ge(z_ps[l], run + 1)
                                act.activation(BZ[0:R, l], pgh(l, R), ACT.Copy).then_inc(z_sb[l], 1)
                        if c == 3 and k == 6 and known(i, 0, NSC):
                            for l in range(NL):
                                act.wait_ge(gate_ps[l], i + 1)
                                need(act, gsil_sb[l], i)
                                act.activation(GT[:, l * LH:(l + 1) * LH].rearrange("p h c -> p (h c)"), PG[:, l], ACT.Tanh, scale=0.5).then_inc(gt_sb[l], 1)
                        if c == 2 and k == 3 and known(i - 2, 0, NSC):
                            for l in range(NL):
                                act.wait_ge(ogt_ps[l], i - 1)
                                need(act, wo_ps, i - 2)
                                act.activation(OGT[:, l * LH:(l + 1) * LH], pgh(l), ACT.Copy).then_inc(ogt_sb[l], 1)
                        if do_prep and k == 7:
                            for l in range(NL):
                                act.wait_ge(ss_ps[l], prep + 1)
                                need(act, e2_sb[l], prep)
                                act.activation(EX[:, l], PD[l].rearrange("p (h t) -> p h t", h=LH), ACT.Exp).then_inc(e_sb[l], 1)
                        if do_prep and k == 11:
                            for l in range(NL):
                                act.wait_ge(kr_ps[l], prep + 1)
                                act.wait_ge(kds_sb[l], prep + 1)
                                need(act, s_ps[l], prep - 1)
                                for h in range(LH):
                                    op = act.activation(KD[:, l, c % 2, h], pgh(l, R)[:, h], ACT.Copy, scale=KDS[0:R, l, h:h + 1])
                                op.then_inc(kd_sb[l], 1)
                        if do_prep and k == 12:
                            for l in range(NL):
                                act.wait_ge(vr_ps[l], prep + 1)
                                act.wait_ge(rt_sb[l], prep + 1)
                                need(act, b_sb[l], prep - 1)
                                for h in range(LH):
                                    op = act.activation(VP[0:R, l, c % 2, h], pgh(l, R)[:, h], ACT.Copy, scale=RT[0:R, l, h:h + 1])
                                op.then_inc(vp_sb[l], 1)
                        if tile_known(i):
                            m = SLOTS * c + k
                            T = TILES * i + m
                            kind, hh, h = tile_of(m)
                            cw = {"q": CWQ[:, h], "k": CWK[:, hh * NHEAD + h], "v": CWV[:, hh * NHEAD + h]}[kind]
                            act.wait_ge(proj_ps, T + 1)
                            need(act, kqv_sb, T - 3)
                            act.activation(CY[:, m % 4], ptile(m)[:, 0:P], ACT.Copy, scale=cw[:, 0:1]).then_inc(tap0_sb, 1)

                all_steps(act, program)

            @block.vector
            def _(dve):
                def tap(j, m, s):
                    T = TILES * j + m
                    kind, hh, h = tile_of(m)
                    cw = {"q": CWQ[:, h], "k": CWK[:, hh * NHEAD + h], "v": CWV[:, hh * NHEAD + h]}[kind]
                    dve.wait_ge(tap0_sb, T + 1)
                    need(dve, taps_sb, 3 * T + s - 1)
                    dve.scalar_tensor_tensor(CY[:, m % 4], ptile(m)[:, s:s + P], cw[:, s:s + 1], CY[:, m % 4],
                                             ALU.mult, ALU.add).then_inc(taps_sb, 1)

                def final(j, jh, m):
                    T = TILES * j + m
                    kind, hh, h = tile_of(m)
                    dve.wait_ge(tanh_sb, T + 1)
                    if kind != "v":
                        for l in range(NL):
                            need(dve, ks_ps[l], CPS * (j - 1))
                    if kind == "v":
                        to = VT[:, jh, h, :, CT * hh:CT * hh + CT]
                    elif kind == "k":
                        to = KQ[:, jh, h, :, CT * hh:CT * hh + CT]
                    else:
                        to = KQ[:, jh, h, :, R:P]
                    v = lambda b: b[:, m % 4].rearrange("p (c t) -> p c t", c=CPS)
                    dve.scalar_tensor_tensor(to, v(CTH), 1.0, v(CY), ALU.add, ALU.mult).then_inc(kqv_sb, 1)

                def inv_out(w, k, l):
                    kind = STAGES[k]
                    if kind == "X":
                        return
                    dve.wait_ge(inv_ps[l], SLOTS * w + k + 1)
                    base, _, to = stage_bufs(k, l)
                    if kind[0] == "W":
                        dve.tensor_tensor(WB[:, l], inv(l), over(merge[int(kind[1])], [R, LH, R], 1), ALU.mult).then_inc(inv_sb[l], 1)
                    else:
                        if k == 13:
                            need(dve, z_ps[l], w)
                        dve.tensor_tensor(to[:, l], base[:, l], inv(l), ALU.subtract).then_inc(inv_sb[l], 1)

                def program(i, half, c):
                    n = 4 * i + c
                    prep, invn, run = n - 4, n - 5, n - 6
                    do_prep, do_inv, do_run = (known(w, 0, NCH) for w in (prep, invn, run))
                    for k in range(SLOTS):
                        j, jh, m = lagged(i, half, SLOTS * c + k - 1)
                        taps = tile_known(j)
                        if taps:
                            tap(j, m, 1)
                        if do_inv:
                            inv_out(invn, k, 0)
                        if taps:
                            tap(j, m, 2)
                        if do_inv:
                            inv_out(invn, k, 1)
                        if taps:
                            tap(j, m, 3)
                        if do_run and k == 0:
                            for l in range(NL):
                                dve.wait_ge(ks_ps[l], run + 1)
                                dve.wait_ge(vp_sb[l], run + 1)
                                need(dve, s_ps[l], run)
                                for h in range(LH):
                                    op = dve.scalar_tensor_tensor(BZ[:, l, h], pgh(l)[:, h], HEADD[:, run, l * LH + h:l * LH + h + 1],
                                                                  VP[:, l, c % 2, h], ALU.mult, ALU.add)
                                op.then_inc(b_sb[l], 1)
                        if do_run and k == (6 if c == 2 else 5):
                            for l in range(NL):
                                dve.wait_ge(s_ps[l], run + 1)
                                for h in range(LH):
                                    hd = l * LH + h
                                    op = dve.scalar_tensor_tensor(S[:, hd], S[:, hd], WHOLE[:, run, hd:hd + 1], pgh(l)[:, h],
                                                                  ALU.mult, ALU.add)
                                op.then_inc(s_sb[l], 1)
                        if c == 2 and known(i - 2, 0, NSC):
                            q = i - 2
                            if k == 1:
                                dve.wait_ge(sso_sb, q + 1)
                                need(dve, fb_sb, q)
                                dve.tensor_scalar(FA[:, :], QSE[:, half], EPS_RMS * P, None, ALU.mult).then_inc(fa_sb, 1)
                                dve.wait_ge(fa_sb, 2 * q + 1)
                                dve.scalar_tensor_tensor(FA[:, :], SSO[:, :], 1.0 / P, FA[:, :], ALU.mult, ALU.add).then_inc(fa_sb, 1)
                            if k == 2:
                                dve.wait_ge(fb_sb, q + 1)
                                dve.wait_ge(gsil_sb[1], q + 1)
                                need(dve, ogt_ps[1], q)
                                for h in range(NHEAD):
                                    op = dve.scalar_tensor_tensor(OG[:, h], PO[:, h], FB[:, h:h + 1], GSIL[:, half, h], ALU.mult, ALU.mult)
                                op.then_inc(og_sb, 1)
                            if k == 5:
                                dve.wait_ge(wo_ps, q + 1)
                                dve.wait_ge(xres_in[half], 8 * (q + 2 - half) if not isinstance(q, int) else 16 * ((q + 2) // 2))
                                dve.tensor_tensor(YL[:, :], PG[:, 0, 0:P], XRES[:, half], ALU.add).then_inc(y_sb, 1)
                                dve.wait_ge(y_sb, q + 1)
                                dve.bn_stats(ST[:, :], YL[:, :]).then_inc(st_sb, 1)
                                dve.wait_ge(st_sb, q + 1)
                                dve.memset(spare[:, :], 0.0)
                                dve.bn_aggr(MV[:, :], ST[:, :]).then_inc(mv_sb, 1)
                                dve.wait_ge(mv_sb, 2 * q + 1)
                                dve.tensor_scalar(MV[:, 1:2], MV[:, 1:2], EPS_LN, None, ALU.add).then_inc(mv_sb, 1)
                            if k == 10:
                                dve.wait_ge(rs_sb, q + 1)
                                need(dve, x1_out[half], 8 * (q - half) if not isinstance(q, int) else 16 * (q // 2))
                                dve.tensor_scalar(X1[:, half], YL[:, :], MV[:, 0:1], RS[:, 0:1], ALU.subtract, ALU.mult).then_inc(x1_sb, 1)
                        if c == 3 and k == 6 and known(i, 0, NSC):
                            for l in range(NL):
                                dve.wait_ge(gt_sb[l], i + 1)
                                dve.scalar_tensor_tensor(GSIL[:, half, l * LH:(l + 1) * LH].rearrange("p h c -> p (h c)"), GT[:, l * LH:(l + 1) * LH].rearrange("p h c -> p (h c)"), 1.0, PG[:, l],
                                                         ALU.add, ALU.mult).then_inc(gsil_sb[l], 1)
                        if do_prep and k == 7:
                            for l in range(NL):
                                dve.wait_ge(e_sb[l], prep + 1)
                                need(dve, rt_sb[l], prep)
                                dve.tensor_scalar(SSE[:, l], PSS[l], EPS_L2, None, ALU.add).then_inc(sse_sb[l], 1)
                                rows = slice(CT * c, CT * c + CT)
                                dve.tensor_scalar(QSE[rows, 1 - half, l * LH:(l + 1) * LH], PSQ[l][rows], EPS_L2, None, ALU.add).then_inc(sse_sb[l], 1)
                                dve.wait_ge(sse_sb[l], 2 * prep + 1)
                                need(dve, kds_sb[l], prep)
                                dve.reciprocal(R2[0:R, l], SSE[0:R, l]).then_inc(r2_sb[l], 1)
                        if do_prep and k == 10:
                            for l in range(NL):
                                dve.wait_ge(kk_ps[l], prep + 1)
                                dve.wait_ge(em_sb[l], prep + 1)
                                need(dve, o_ps[l], prep - 1)
                                dve.tensor_tensor(U[0:R, l, c % 2], pgh(l, R), EM[0:R, l], ALU.mult).then_inc(u_sb[l], 1)
                        if c == 3 and k == 8 and known(i + 1, 1, NSC):
                            x_in(i + 1, 1 - half)
                        j, jh, m = lagged(i, half, SLOTS * c + k - 3)
                        if tile_known(j):
                            final(j, jh, m)

                def x_in(i, half):
                    dve.wait_ge(xt_ps, i + 1)
                    dve.tensor_copy(XT[:, half, HALO:], PG[:, 0, 0:P]).then_inc(xt_sb, 1)
                    dve.tensor_scalar(XT[:, half, 0:HALO], XT[:, 1 - half, P:], C[:, bass.ds(C_KEEP + i % NSC, 1)],
                                      None, ALU.mult).then_inc(xt_sb, 1)

                dve.memset(XT[:, :, :], 0.0).then_inc(ready, 1)
                dve.memset(S[:, :, :], 0.0).then_inc(ready, 1)
                for l in range(NL):
                    for b in range(2):
                        dve.memset(VP[R:P, l, b], 0.0).then_inc(ready, 1)
                        for h in range(LH):
                            dve.tensor_copy(U[R:P, l, b, h, R:P], ident[R:P, R:P]).then_inc(ready, 1)
                dve.wait_ge(ready, READY)
                x_in(0, 0)
                all_steps(dve, program)

            @block.gpsimd
            def _(pool):
                def program(i, half, c):
                    n = 4 * i + c
                    prep = n - 4
                    run = n - 6
                    sc = 1 - half
                    if known(prep, 0, NCH):
                        for l in range(NL):
                            heads = slice(l * LH, (l + 1) * LH)
                            pool.wait_ge(kqv_sb, TILES * i)
                            need(pool, ss_ps[l], prep)
                            kq = KQ[:, sc, heads, c]
                            pool.tensor_tensor(SQ[:, l], kq, kq, ALU.mult).then_inc(sq_sb[l], 1)
                            need(pool, ss_ps[l], prep)
                            pool.wait_ge(sq_sb[l], prep + 1)
                            pool.tensor_tensor(GM[R:P, l], over(G[R:P, prep, heads], [CT, LH, CT], 2),
                                               over(upto[:, 0:CT], [CT, LH, CT], 1), ALU.mult).then_inc(gm_sb[l], 1)
                            pool.wait_ge(gm_sb[l], prep + 1)
                    if c == 2 and known(i - 2, 0, NSC):
                        pool.wait_ge(fa_sb, 2 * (i - 1))
                        need(pool, og_sb, i - 2)
                        pool.tensor_tensor(FB[:, :], FA[:, :], mhalf[:, :], ALU.pow).then_inc(fb_sb, 1)
                    if known(prep, 0, NCH):
                        for l in range(NL):
                            heads = slice(l * LH, (l + 1) * LH)
                            pool.wait_ge(sse_sb[l], 2 * prep + 1)
                            need(pool, vp_sb[l], prep)
                            pool.tensor_tensor(RT[:, l], SSE[:, l], half4[:, 0:LH], ALU.pow).then_inc(rt_sb[l], 1)
                            pool.wait_ge(r2_sb[l], prep + 1)
                            pool.tensor_tensor(S1[0:R, l], R2[0:R, l], BETA[0:R, prep, heads], ALU.mult).then_inc(s1_sb[l], 1)
                            need(pool, kd_sb[l], prep)
                            pool.tensor_tensor(KDS[0:R, l], R2[0:R, l], TAIL[0:R, prep, heads], ALU.mult).then_inc(kds_sb[l], 1)
                            pool.wait_ge(e_sb[l], prep + 1)
                            pool.wait_ge(s1_sb[l], prep + 1)
                            need(pool, em_sb[l], prep)
                            pool.tensor_tensor(E2[:, l], EX[:, l], over(S1[0:R, l], [R, LH, CT], 2), ALU.mult).then_inc(e2_sb[l], 1)
                            pool.wait_ge(e2_sb[l], prep + 1)
                            need(pool, u_sb[l], prep)
                            for s in range(P // CT):
                                op = pool.tensor_tensor(EM[0:R, l, :, CT * s:CT * s + CT], E2[:, l],
                                                        over(earlier[:, CT * s:CT * s + CT], [R, LH, CT], 1), ALU.mult)
                            op.then_inc(em_sb[l], 1)
                    if c == 2 and known(i - 2, 0, NSC):
                        pool.wait_ge(mv_sb, 2 * (i - 1))
                        need(pool, x1_sb, i - 2)
                        pool.tensor_tensor(RS[:, :], MV[:, 1:2], mhalf[:, 0:1], ALU.pow).then_inc(rs_sb, 1)
                    if known(prep, 0, NCH):
                        for l in range(NL):
                            pool.wait_ge(u_sb[l], prep + 1)
                            need(pool, y1_sb[l], prep)
                            pool.tensor_tensor(EM[0:R, l, :, 0:R], U[0:R, l, c % 2, :, 0:R], over(first, [R, LH, R], 1), ALU.mult).then_inc(seed_sb[l], 1)
                            pool.wait_ge(seed_sb[l], prep + 1)
                            need(pool, inv_sb[l], SLOTS * (prep - 1) + 4)
                            pool.tensor_tensor(Y1[:, l], EM[0:R, l, :, 0:R], over(ident[0:R, 0:R], [R, LH, R], 1), ALU.add).then_inc(y1_sb[l], 1)

                all_steps(pool, program)



def ffn_part(nc, x1, cent, Wp, bp, W1, b1, W2, b2, consts, out):
    ctx = ExitStack()
    with ctx:
        def sb(name, shape):
            return ctx.enter_context(nc.sbuf_tensor(name, shape, F32))

        def pb(name, shape):
            return ctx.enter_context(nc.psum_tensor(name, shape, F32))

        def sem(name):
            return ctx.enter_context(nc.semaphore(name))

        of = out.rearrange("b t d -> (b t) d")
        NI = NB * NT // FT
        C = sb("Cf", [P, C_ALL])
        ident = C[:, C_ID:C_ID + P]
        lower = C[:, C_LOWER:C_LOWER + NE * NE]
        W1S = sb("W1S", [P, NE, FF])
        W2S = sb("W2S", [P, FC, P])
        B1S = sb("B1S", [P, FC])
        B2S = sb("B2S", [NE, P])
        WP = sb("WP", [P, P])
        BP = sb("BP", [P, 1])
        CEN = sb("CEN", [NE, P])
        CSQ = sb("CSQ", [NE, P])
        cs = sb("cs", [NE, 4])
        CT_ = sb("CT_", [P, NE])
        CTQ = sb("CTQ", [P, NE])
        CNS = sb("CNS", [P, 2, NE])
        hf = sb("hf", [P, FQ * NE])
        mh = sb("mh", [P, FQ])
        onesf = sb("onesf", [P, P])
        XI = sb("XI", [P, 2, FQ, P])
        XIT = sb("XIT", [P, 2, FT])
        XH = sb("XH", [P, FT])
        XH2 = sb("XH2", [P, FT])
        r1 = {k: sb("r1" + k, [P, FQ]) for k in ("nrm", "scl", "sc2", "xns", "omx", "fm", "sm", "rs")}
        r8 = {k: sb("r8" + k, [P, FQ, NE]) for k in ("dot", "d", "den", "rd", "arg", "am", "pr", "sq", "f", "rf", "rr", "rank", "sel", "w")}
        CMP = sb("CMP", [P, FQ, NE, NE])
        CM2 = sb("CM2", [P, FQ, NE, NE])
        COMB = sb("COMB", [P, 2, FQ, NE])
        CBT = sb("CBT", [NE, FT])
        ACC = sb("ACC", [P, 2, FQ, P])
        HS = sb("HS", [P, 3, FT])
        ST = sb("STf", [P, FQ, 6])
        MV = sb("MVf", [P, FQ, 2])
        VE = sb("VE", [P, FQ])
        RS = sb("RSf", [P, FQ])
        spare = sb("sparef", [P, 1])
        OUT = sb("OUT", [P, 2, FQ, P])

        PT = pb("PT", [P, 512])
        PR = pb("PR", [P, 512])
        PQ = pb("PQ", [P, FQ, 16])
        PC = pb("PC", [P, 512])
        PH = pb("PH", [P, 2, 512])
        PY = pb("PY", [P, 2, 512])

        w_in, x_in, o_out = sem("w_inf"), [sem(f"xi_in{b}") for b in range(2)], [sem(f"o_out{b}") for b in range(2)]
        ms, cen, cen_ps = sem("ms"), sem("cen"), sem("cen_ps")
        (xt_ps, xt_sb, xh_ps, xh_sb, xh2_sb, dots_ps, dots_sb, pow_sb, rt, comb_sb, ct_ps, ct_sb, b2_ps, acc_sb,
         h_ps, h_sb, y_ps, ln, rs_sb, o_sb) = (sem(n) for n in (
             "fxt_ps", "fxt_sb", "xh_ps", "xh_sb", "xh2_sb", "dots_ps", "dots_sb", "pow_sb", "rt", "comb_sb", "ct_ps",
             "ct_sb", "b2_ps", "acc_sb", "h_ps", "h_sb", "y_ps", "ln", "frs_sb", "o_sb"))
        NWF = 8
        ROUTE = 31
        PR_READY = 18
        LNS = 9

        with nc.Block() as block:
            @block.sync
            def _(sp):
                sp.dma_start(C[:, :], consts).then_inc(w_in, 16)
                sp.dma_start(CEN[:, :], cent).then_inc(w_in, 16)
                sp.dma_start(WP[:, :], Wp).then_inc(w_in, 16)
                sp.dma_start(BP[:, :], bp.unsqueeze(1)).then_inc(w_in, 16)
                sp.dma_start(W1S[:, :, :], W1.rearrange("e d f -> d e f")).then_inc(w_in, 16)
                sp.dma_start(B1S[:, :], b1.rearrange("e (c p) -> p (e c)", p=P), allow_slow_non_contiguous=True).then_inc(w_in, 16)
                sp.dma_start(W2S[:, :, :], W2.rearrange("e (c p) d -> p (e c) d", p=P)).then_inc(w_in, 16)
                sp.dma_start(B2S[:, :], b2).then_inc(w_in, 16)

                def load(u, b):
                    sp.dma_start(XI[:, b], x1[bass.ds(u * FT, FT)].rearrange("(q p) d -> p q d", p=P)).then_inc(x_in[b], 16)

                def step(t, b, more):
                    u = 2 * t + b
                    if more:
                        sp.wait_ge(xt_ps, u) if not isinstance(u, int) or u > 0 else None
                        sp.wait_ge(acc_sb, (NE + 1) * u - NE) if not isinstance(u, int) or u > 0 else None
                        load(u + 1, 1 - b)
                    sp.wait_ge(o_sb, u + 1)
                    sp.dma_start(of[bass.ds(u * FT, FT)].rearrange("(q p) d -> p q d", p=P), OUT[:, b]).then_inc(o_out[b], 16)

                load(0, 0)
                step(0, 0, True)
                step(0, 1, True)
                with sp.Fori(1, NI // 2 - 1) as t:
                    step(t, 0, True)
                    step(t, 1, True)
                step(NI // 2 - 1, 0, True)
                step(NI // 2 - 1, 1, False)
                for b in range(2):
                    sp.wait_ge(o_out[b], 16 * NI // 2)

            @block.tensor
            def _(pe):
                pe.wait_ge(w_in, 16 * NWF)
                pe.wait_ge(ms, 3)
                pe.wait_ge(cen, 4)
                pe.transpose(PC[:, 0:NE], CEN[:, :], ident[0:NE, 0:NE]).then_inc(cen_ps, 1)
                pe.wait_ge(cen, 6)
                pe.matmul(PC[:, 16:16 + NE], onesf[:, :], CTQ[:, :], start=True, stop=True).then_inc(cen_ps, 1)

                def h_mm(u, b, f):
                    F = FC * u + f
                    need(pe, h_sb, F - 1)
                    pe.matmul(PH[:, f % 2], W1S[:, f // 4, (f % 4) * P:(f % 4 + 1) * P], XIT[:, b], start=True, stop=True).then_inc(h_ps, 1)

                def y_mm(u, f):
                    F = FC * u + f
                    e = f // 4
                    pe.wait_ge(h_sb, F + 1)
                    if f % 4 == 0:
                        need(pe, acc_sb, (NE + 1) * u + e if e >= 2 else (NE + 1) * u - 1 + e)
                    for q in range(FQ):
                        mm = pe.matmul(PY[:, e % 2, q * P:(q + 1) * P], HS[:, hs_slot(f), q * P:(q + 1) * P], W2S[:, f],
                                       start=(f % 4 == 0 and q == 0), stop=(f % 4 == 3), skip_group_check=True)
                    mm.then_inc(y_ps, 1)

                def step(t, b):
                    u = 2 * t + b
                    pe.wait_ge(x_in[b], 16 * (t + 1))
                    for q in range(FQ):
                        mm = pe.transpose(PT[:, q * P:(q + 1) * P], XI[:, b, q], ident)
                    mm.then_inc(xt_ps, 1)
                    pe.wait_ge(xt_sb, u + 1)
                    pe.matmul(PR[:, :], WP[:, :], XIT[:, b], start=True, stop=True).then_inc(xh_ps, 1)
                    h_mm(u, b, 0)
                    h_mm(u, b, 1)
                    pe.wait_ge(xh2_sb, u + 1)
                    pe.wait_ge(cen, 7)
                    for q in range(FQ):
                        pe.matmul(PQ[:, q, 0:NE], XH[:, q * P:(q + 1) * P], CT_[:, :], start=True, stop=True)
                        mm = pe.matmul(PQ[:, q, NE:NE + 1], XH2[:, q * P:(q + 1) * P], onesf[:, 0:1], start=True, stop=True)
                    mm.then_inc(dots_ps, 1)
                    for f in range(FC):
                        if f == 4:
                            pe.wait_ge(comb_sb, u + 1)
                            for q in range(FQ):
                                mm = pe.transpose(PC[0:NE, q * P:(q + 1) * P], COMB[:, b, q], ident)
                            mm.then_inc(ct_ps, 1)
                            pe.wait_ge(ct_sb, u + 1)
                            for q in range(FQ):
                                mm = pe.matmul(PC[:, q * P:(q + 1) * P], CBT[:, q * P:(q + 1) * P], B2S[:, :], start=True, stop=True)
                            mm.then_inc(b2_ps, 1)
                        y_mm(u, f)
                        if f + 2 < FC:
                            h_mm(u, b, f + 2)

                step(0, 0)
                step(0, 1)
                with pe.Fori(1, NI // 2) as t:
                    step(t, 0)
                    step(t, 1)

            @block.scalar
            def _(act):
                act.wait_ge(w_in, 16 * NWF)
                act.activation(CSQ[:, :], CEN[:, :], ACT.Square, accum_out=cs[:, 0:1]).then_inc(cen, 1)

                def gelu(u, f):
                    F = FC * u + f
                    act.wait_ge(h_ps, F + 1)
                    need(act, y_ps, F - 1)
                    act.activation(HS[:, hs_slot(f)], PH[:, f % 2], ACT.Gelu, bias=B1S[:, f:f + 1]).then_inc(h_sb, 1)

                def step(t, b):
                    u = 2 * t + b
                    act.wait_ge(xh_ps, u + 1)
                    need(act, dots_ps, u)
                    act.activation(XH[:, :], PR[:, :], ACT.Identity, bias=BP[:, 0:1]).then_inc(xh_sb, 1)
                    act.activation(XH2[:, :], PR[:, :], ACT.Square, bias=BP[:, 0:1]).then_inc(xh2_sb, 1)
                    for f in range(FC):
                        gelu(u, f)

                step(0, 0)
                step(0, 1)
                with act.Fori(1, NI // 2) as t:
                    step(t, 0)
                    step(t, 1)

            @block.gpsimd
            def _(pool):
                pool.memset(hf[:, :], 0.5).then_inc(ms, 1)
                pool.memset(onesf[:, :], 1.0).then_inc(ms, 1)
                pool.memset(mh[:, :], -0.5).then_inc(ms, 1)
                pool.wait_ge(ms, 3)
                pool.wait_ge(cen, 1)
                pool.tensor_tensor(cs[:, 1:2], cs[:, 0:1], hf[0:NE, 0:1], ALU.pow).then_inc(cen, 1)
                flat = lambda t: t[:, :, :].rearrange("p a b -> p (a b)")

                def step(u):
                    pool.wait_ge(dots_sb, 2 * u + 2)
                    pool.tensor_tensor(r1["nrm"][:, :], r1["sc2"][:, :], hf[:, 0:FQ], ALU.pow).then_inc(pow_sb, 1)
                    pool.wait_ge(rt, ROUTE * (u + 1) + PR_READY)
                    pool.tensor_tensor(flat(r8["sq"]), flat(r8["pr"]), hf[:, :], ALU.pow).then_inc(pow_sb, 1)
                    pool.wait_ge(ln, LNS * (u + 1))
                    pool.tensor_tensor(RS[:, :], VE[:, :], mh[:, :], ALU.pow).then_inc(rs_sb, 1)

                with pool.Fori(0, NI) as u:
                    step(u)

            @block.vector
            def _(dve):
                dve.wait_ge(cen, 2)
                dve.tensor_scalar(cs[:, 2:3], cs[:, 1:2], 1e-7, None, ALU.max).then_inc(rt, 1)
                dve.wait_ge(rt, 1)
                dve.reciprocal(cs[:, 3:4], cs[:, 2:3]).then_inc(rt, 1)
                dve.wait_ge(rt, 2)
                dve.tensor_scalar(cs[:, 3:4], cs[:, 3:4], MAX_NORM, 1.0, ALU.mult, ALU.min).then_inc(cen, 1)
                dve.wait_ge(cen, 3)
                dve.tensor_scalar(CEN[:, :], CEN[:, :], cs[:, 3:4], None, ALU.mult).then_inc(cen, 1)
                dve.wait_ge(cen_ps, 1)
                dve.tensor_copy(CT_[:, :], PC[:, 0:NE]).then_inc(cen, 1)
                dve.wait_ge(cen, 5)
                dve.tensor_tensor(CTQ[:, :], CT_[:, :], CT_[:, :], ALU.mult).then_inc(cen, 1)
                dve.wait_ge(cen_ps, 2)
                dve.tensor_scalar(CNS[:, 0], PC[:, 16:16 + NE], 0.99, None, ALU.min).then_inc(cen, 1)
                dve.wait_ge(cen, 7)
                dve.tensor_scalar(CNS[:, 1], CNS[:, 0], -1.0, 1.0, ALU.mult, ALU.add).then_inc(rt, ROUTE - 2)
                dve.wait_ge(rt, ROUTE)

                def experts_out(u, b, e):
                    dve.wait_ge(y_ps, FC * u + 4 * (e + 1))
                    for q in range(FQ):
                        op = dve.scalar_tensor_tensor(ACC[:, b, q], PY[:, e % 2, q * P:(q + 1) * P], COMB[:, b, q, e:e + 1],
                                                      ACC[:, b, q], ALU.mult, ALU.add)
                    op.then_inc(acc_sb, 1)

                def step(t, b):
                    u = 2 * t + b
                    dve.wait_ge(xt_ps, u + 1)
                    dve.tensor_copy(XIT[:, b], PT[:, :]).then_inc(xt_sb, 1)
                    route_all(dve, u, b)
                    dve.wait_ge(ct_ps, u + 1)
                    dve.tensor_copy(CBT[:, :], PC[0:NE, :]).then_inc(ct_sb, 1)
                    dve.wait_ge(b2_ps, u + 1)
                    dve.tensor_tensor(ACC[:, b].rearrange("p q d -> p (q d)"), PC[:, :], XI[:, b].rearrange("p q d -> p (q d)"),
                                      ALU.add).then_inc(acc_sb, 1)
                    for e in range(NE):
                        dve.wait_ge(acc_sb, (NE + 1) * u + e + 1)
                        experts_out(u, b, e)
                    base = LNS * u
                    dve.wait_ge(acc_sb, (NE + 1) * (u + 1))
                    for q in range(FQ):
                        dve.bn_stats(ST[:, q], ACC[:, b, q]).then_inc(ln, 1)
                    dve.wait_ge(ln, base + FQ)
                    dve.memset(spare[:, :], 0.0)
                    for q in range(FQ):
                        dve.bn_aggr(MV[:, q], ST[:, q]).then_inc(ln, 1)
                    dve.wait_ge(ln, base + 8)
                    dve.tensor_scalar(VE[:, :], MV[:, :, 1], EPS_LN, None, ALU.add).then_inc(ln, 1)
                    dve.wait_ge(rs_sb, u + 1)
                    if not isinstance(t, int) or t > 0:
                        dve.wait_ge(o_out[b], 16 * t)
                    for q in range(FQ):
                        op = dve.tensor_scalar(OUT[:, b, q], ACC[:, b, q], MV[:, q, 0:1], RS[:, q:q + 1], ALU.subtract, ALU.mult)
                    op.then_inc(o_sb, 1)

                def route_all(dve, u, b):
                    count = [ROUTE * u + ROUTE]
                    total = [0]

                    def then(op, k=1):
                        op.then_inc(rt, k)
                        total[0] += k
                        dve.wait_ge(rt, count[0] + total[0])

                    v1 = lambda k: r1[k][:, :]
                    v8 = lambda k: r8[k][:, :, :]
                    w1 = lambda k: over(r1[k][:, :], [P, FQ, NE], 2)
                    c8 = lambda m: over(CNS[:, m], [P, FQ, NE], 1)
                    dve.wait_ge(dots_ps, u + 1)
                    dve.tensor_copy(v8("dot"), PQ[:, :, 0:NE]).then_inc(dots_sb, 1)
                    dve.tensor_copy(v1("sc2"), PQ[:, :, NE]).then_inc(dots_sb, 1)
                    dve.wait_ge(pow_sb, 2 * u + 1)
                    then(dve.tensor_scalar(v1("scl"), v1("nrm"), 1e-7, None, ALU.max))
                    then(dve.reciprocal(v1("fm"), v1("scl")))
                    then(dve.tensor_scalar(v1("scl"), v1("fm"), MAX_NORM, 1.0, ALU.mult, ALU.min))
                    then(dve.tensor_tensor(v1("xns"), v1("scl"), v1("scl"), ALU.mult))
                    then(dve.tensor_tensor(v1("xns"), v1("xns"), v1("sc2"), ALU.mult))
                    then(dve.tensor_scalar(v1("xns"), v1("xns"), 0.99, None, ALU.min))
                    then(dve.tensor_scalar(v1("omx"), v1("xns"), -1.0, 1.0, ALU.mult, ALU.add))
                    then(dve.tensor_tensor(v8("d"), v8("dot"), w1("scl"), ALU.mult))
                    then(dve.scalar_tensor_tensor(v8("d"), v8("d"), -2.0, w1("xns"), ALU.mult, ALU.add))
                    then(dve.tensor_tensor(v8("d"), v8("d"), c8(0), ALU.add))
                    then(dve.tensor_tensor(v8("den"), c8(1), w1("omx"), ALU.mult))
                    then(dve.tensor_scalar(v8("den"), v8("den"), 1e-7, None, ALU.add))
                    then(dve.reciprocal(v8("rd"), v8("den")))
                    then(dve.tensor_scalar(v8("d"), v8("d"), 0.0, 2.0, ALU.max, ALU.mult))
                    then(dve.tensor_tensor(v8("rd"), v8("rd"), v8("d"), ALU.mult))
                    then(dve.tensor_scalar(v8("arg"), v8("rd"), 1.0, 1.0 + 1e-7, ALU.add, ALU.max))
                    then(dve.tensor_scalar(v8("am"), v8("arg"), -1.0, None, ALU.add))
                    then(dve.scalar_tensor_tensor(v8("pr"), v8("arg"), 1.0, v8("am"), ALU.add, ALU.mult))
                    assert total[0] == PR_READY
                    near = over(v8("arg"), [P, FQ, NE, NE], 2)
                    own = over(v8("arg"), [P, FQ, NE, NE], 3)
                    then(dve.tensor_tensor(CMP[:, :, :, :], near, own, ALU.is_equal))
                    then(dve.tensor_tensor(CMP[:, :, :, :].rearrange("p q a b -> p q (a b)"), CMP[:, :, :, :].rearrange("p q a b -> p q (a b)"),
                                           over(lower, [P, FQ, NE * NE], 1), ALU.mult))
                    then(dve.tensor_tensor(CM2[:, :, :, :], near, own, ALU.is_lt))
                    then(dve.tensor_tensor(CMP[:, :, :, :], CMP[:, :, :, :], CM2[:, :, :, :], ALU.add))
                    then(dve.tensor_reduce(v8("rank"), CMP[:, :, :, :], AX.X, ALU.add))
                    then(dve.tensor_scalar(v8("sel"), v8("rank"), 2.0, None, ALU.is_lt))
                    dve.wait_ge(pow_sb, 2 * u + 2)
                    then(dve.tensor_tensor(v8("f"), v8("arg"), v8("sq"), ALU.add))
                    then(dve.tensor_reduce(v1("fm"), v8("f"), AX.X, ALU.min))
                    then(dve.reciprocal(v8("rf"), v8("f")))
                    then(dve.tensor_tensor(v8("rr"), v8("rf"), w1("fm"), ALU.mult))
                    then(dve.tensor_tensor(v8("w"), v8("rr"), v8("sel"), ALU.mult))
                    then(dve.tensor_reduce(v1("sm"), v8("w"), AX.X, ALU.add))
                    then(dve.reciprocal(v1("rs"), v1("sm")))
                    assert total[0] == ROUTE
                    dve.tensor_tensor(COMB[:, b], v8("w"), w1("rs"), ALU.mult).then_inc(comb_sb, 1)

                step(0, 0)
                step(0, 1)
                with dve.Fori(1, NI // 2) as t:
                    step(t, 0)
                    step(t, 1)


def hs_slot(f):
    return f % 2


_INS = ['L0_attn_x', 'L0_attn_Wq', 'L0_attn_Wk', 'L0_attn_Wv', 'L0_attn_Wb', 'L0_attn_Wa', 'L0_attn_A_log',
        'L0_attn_dt_bias', 'L0_attn_conv_q', 'L0_attn_conv_k', 'L0_attn_conv_v', 'L0_attn_Wg', 'L0_attn_rms_weight',
        'L0_attn_Wo', 'L0_ffn_centroids', 'L0_ffn_Wp', 'L0_ffn_bp', 'L0_ffn_W1', 'L0_ffn_b1', 'L0_ffn_W2', 'L0_ffn_b2']


def kernel(**inputs):
    import numpy as np
    import concourse.bacc as bacc
    from concourse.bass_utils import run_bass_kernel_spmd

    nc = bacc.Bacc("TRN2", target_bir_lowering=False, num_devices=1, dynamic_dma_scratch_size=1024)
    arrays, args = {}, []
    for name in _INS:
        a = np.ascontiguousarray(inputs[name])
        arrays[f"in_{name}"] = a
        args.append(nc.dram_tensor(f"in_{name}", a.shape, mybir.dt.from_np(a.dtype), kind="ExternalInput").ap())
    a = attn_consts()
    arrays["in_consts"] = a
    consts = nc.dram_tensor("in_consts", a.shape, F32, kind="ExternalInput").ap()
    x1 = nc.dram_tensor("x1", (NB * NT, P), F32, kind="Internal").ap()
    out = nc.dram_tensor("out_0", (NB, NT, P), F32, kind="ExternalOutput").ap()
    attention_part(nc, *args[:14], consts, x1)
    ffn_part(nc, x1, *args[14:], consts, out)
    r = run_bass_kernel_spmd(nc, [arrays], core_ids=[0])
    return r.results[0]["out_0"]
```
